# Optimizing a Trainium2 kernel written in Bass

```python
import numpy as np
import jax
import jax.numpy as jnp

def _softmax(x, axis=-1):
    return jax.nn.softmax(x, axis=axis)

def _gelu(x):
    return jax.nn.gelu(x, approximate=True)

def _silu(x):
    return jax.nn.silu(x)

def _sigmoid(x):
    return jax.nn.sigmoid(x)

def _layernorm(x, axis=-1, eps=1e-05):
    m = jnp.mean(x, axis=axis, keepdims=True)
    v = jnp.var(x, axis=axis, keepdims=True)
    return (x - m) / jnp.sqrt(v + eps)

def _scatter_add(tgt, idx, src, axis=0):
    return tgt.at[idx].add(src)

def _segment_sum(src, seg, n):
    return jax.ops.segment_sum(src, seg, n)
kernel_name = 'mk_adj_resnorm_d1_adj_r2_d556c5'

def setup_inputs(seed: int=0):
    np.random.seed(seed)
    _w = jnp.asarray

    def _rec_inputs():
        import jax
        import jax.numpy as jnp
        _gk = jax.random.key(seed)
        x = -0.0001538 + 1 * jax.random.normal(jax.random.fold_in(_gk, 1), (64, 128, 384), jnp.float32)
        _w = (1.0 + jnp.arange(128, dtype=jnp.float32)) ** (-0.5)
        _w = _w / _w.mean()
        _pij = jnp.clip(0.03125 * _w[:, None] * _w[None, :], 0.0, 1.0)
        _a = jax.random.uniform(jax.random.fold_in(_gk, 2), (64, 128, 128)) < _pij
        _a = jnp.logical_or(_a, jnp.swapaxes(_a, -1, -2))
        _a = jnp.logical_or(_a, jnp.eye(128, dtype=bool))
        _af = _a.astype(jnp.float32)
        _af = _af * jax.random.uniform(jax.random.fold_in(_gk, 3), (64, 128, 128), jnp.float32, 0.05, 4.42607)
        adj = _af
        return (x, adj)
    x, adj = _rec_inputs()

    def _L0_gnn_setup():
        import jax, jax.numpy as jnp
        import numpy as np
        NUM_HEADS = 12
        HIDDEN = 384
        HEAD = HIDDEN // NUM_HEADS
        B, N = (16, 256)
        key = jax.random.key(seed)
        ks = jax.random.split(key, 9)
        s = 0.02
        return {'x': jax.random.normal(ks[0], (B, N, HIDDEN), jnp.float32), 'spatial_encoding': jax.random.normal(ks[1], (B, N, N), jnp.float32), 'edge_encoding': jax.random.normal(ks[2], (B, N, N), jnp.float32), 'Wq': jax.random.normal(ks[3], (HIDDEN, HIDDEN), jnp.float32) * s, 'Wk': jax.random.normal(ks[4], (HIDDEN, HIDDEN), jnp.float32) * s, 'Wv': jax.random.normal(ks[5], (HIDDEN, HIDDEN), jnp.float32) * s, 'bv': jax.random.normal(ks[6], (HIDDEN,), jnp.float32) * s, 'Wo': jax.random.normal(ks[7], (HIDDEN, HIDDEN), jnp.float32) * s, 'bo': jax.random.normal(ks[8], (HIDDEN,), jnp.float32) * s}
    _L0_gnn_all = _L0_gnn_setup()
    _L0_gnn_in = {k: v for k, v in _L0_gnn_all.items() if k in ('Wq', 'Wk', 'Wv', 'bv', 'Wo', 'bo')}
    del _L0_gnn_all
    return {'x': x, 'adj': adj, 'L0_gnn_Wq': _L0_gnn_in['Wq'], 'L0_gnn_Wk': _L0_gnn_in['Wk'], 'L0_gnn_Wv': _L0_gnn_in['Wv'], 'L0_gnn_bv': _L0_gnn_in['bv'], 'L0_gnn_Wo': _L0_gnn_in['Wo'], 'L0_gnn_bo': _L0_gnn_in['bo']}

def reference(x, adj, L0_gnn_Wq, L0_gnn_Wk, L0_gnn_Wv, L0_gnn_bv, L0_gnn_Wo, L0_gnn_bo):
    import jax
    import jax.numpy as jnp

    def _L0_gnn_ref(x, spatial_encoding, edge_encoding, Wq, Wk, Wv, bv, Wo, bo):
        import jax, jax.numpy as jnp
        import numpy as np
        NUM_HEADS = 12
        HIDDEN = 384
        HEAD = HIDDEN // NUM_HEADS
        B, N = (16, 256)
        b, n, h = x.shape
        scale = jnp.asarray(HIDDEN, x.dtype) ** (-0.5)
        q = (x @ Wq.T).reshape(b, n, NUM_HEADS, HEAD)
        k = (x @ Wk.T).reshape(b, n, NUM_HEADS, HEAD)
        v = (x @ Wv.T + bv).reshape(b, n, NUM_HEADS, HEAD)
        bias = (spatial_encoding + edge_encoding)[:, None]
        scores = jnp.einsum('bqhd,bkhd->bhqk', q, k) * scale + bias
        row_nonzero = jnp.any(scores != 0, axis=-1, keepdims=True)
        scores = jnp.where(row_nonzero, scores, -jnp.inf)
        p = jax.nn.softmax(scores, axis=-1)
        p = jnp.nan_to_num(p)
        out = jnp.einsum('bhqk,bkhd->bqhd', p, v).reshape(b, n, h)
        return out @ Wo.T + bo
    x = _layernorm(x + _L0_gnn_ref(x, adj, adj, L0_gnn_Wq, L0_gnn_Wk, L0_gnn_Wv, L0_gnn_bv, L0_gnn_Wo, L0_gnn_bo), axis=-1)
    return x

_drawn_inputs = setup_inputs


def setup_inputs(seed=0):
    import zlib

    import numpy as np

    out = dict(_drawn_inputs(seed))
    spreads = {}
    factors = {'L0_gnn_Wq': 8.0, 'L0_gnn_Wk': 8.0, 'L0_gnn_bv': 6.287, 'L0_gnn_bo': 2.985}
    for name, (base, spread) in spreads.items():
        noise = np.random.default_rng([zlib.crc32(name.encode()), seed]).standard_normal(out[name].shape)
        drawn = base * np.exp(spread * noise) if base else spread * noise
        out[name] = jnp.asarray(drawn.astype(out[name].dtype))
    for name, factor in factors.items():
        out[name] = (out[name] * factor).astype(out[name].dtype)
    return out
```

```python
from contextlib import ExitStack

import concourse.bass as bass
from concourse import mybir
from concourse.alu_op_type import AluOpType as ALU

ACT = mybir.ActivationFunctionType
AX = mybir.AxisListType
F32 = mybir.dt.float32

P = 128
NB = 64
HID = 384
HEADS = 12
D = HID // HEADS
KT = HID // P
HPT = P // D
GRP = 4
NG = NB // GRP
BODY = 2 * GRP
STEPS = NB // BODY
EPS = 1e-5
SCALE = float(HID) ** -0.5
DMA = 16


def build(nc, xt, xn, adj, wq, wk, wv, wo, bv, bo, out):
    with ExitStack() as ctx:
        def sb(name, shape, dt=F32):
            return ctx.enter_context(nc.sbuf_tensor(name, shape, dt))

        def ps(name, shape, dt=F32):
            return ctx.enter_context(nc.psum_tensor(name, shape, dt))

        def sem(name):
            return ctx.enter_context(nc.semaphore(name))

        w_q = sb("w_q", [P, KT, HID])
        w_k = sb("w_k", [P, KT, HID])
        w_v = sb("w_v", [P, KT, HID])
        w_o = sb("w_o", [P, KT, HID])
        bv_rows = sb("bv_rows", [P, HID])
        bo_rows = sb("bo_rows", [P, HID])
        ident = sb("ident", [P, P])
        minus_half = sb("minus_half", [P, 1])
        x_t = sb("x_t", [P, 2, KT, GRP * P])
        x_n = sb("x_n", [P, 2, GRP, HID])
        adj_n = sb("adj_n", [P, 2, GRP, P])
        q_t = sb("q_t", [P, 2, KT, GRP * P])
        k_diag = sb("k_diag", [P, 2, GRP, KT, HPT, P])
        v_n = sb("v_n", [P, 2, HID])
        nscores = sb("nscores", [P, 2, HEADS, P])
        probs = sb("probs", [P, 2, HEADS, P])
        probs_t = sb("probs_t", [P, 2, HEADS, P])
        neg_max = sb("neg_max", [P, 2, HEADS])
        row_sum = sb("row_sum", [P, 2, HEADS])
        tree = sb("tree", [P, HEADS, P])
        recip = sb("recip", [P, HEADS])
        guard = sb("guard", [P, HEADS])
        scale_n = sb("scale_n", [P, 2, HID])
        scale_t = sb("scale_t", [P, 2, HID])
        att_t = sb("att_t", [P, 2, KT, P])
        y = sb("y", [P, 2, HID])
        stats = sb("stats", [P, 2, 6])
        mean_var = sb("mean_var", [P, 2, 2])
        var_eps = sb("var_eps", [P, 1])
        rstd = sb("rstd", [P, 2])
        out_n = sb("out_n", [P, 2, GRP, HID])

        scores_ps = [ps(f"scores_ps{m}", [P, HPT, P]) for m in range(KT)]
        pt_ps = [ps(f"pt_ps{i}", [P, HPT, P]) for i in range(2)]
        att_ps = ps("att_ps", [P, 512])
        mm_ps = [ps(f"mm_ps{i}", [P, 512]) for i in range(2)]

        w_in = {n: sem(f"w_in_{n}") for n in ("q", "k", "v", "o", "b")}
        xt_in = [sem(f"xt_in{i}") for i in range(2)]
        xn_in = [sem(f"xn_in{i}") for i in range(2)]
        adj_in = [sem(f"adj_in{i}") for i in range(2)]
        ident_step = sem("ident_step")
        diag_zeroed = [sem(f"diag_zeroed{i}") for i in range(2)]
        proj_done = sem("proj_done")
        k_ready = sem("k_ready")
        q_ready = sem("q_ready")
        scores_done = sem("scores_done")
        biased = sem("biased")
        vproj_done = sem("vproj_done")
        v_ready = sem("v_ready")
        probs_ready = sem("probs_ready")
        turned = sem("turned")
        pt_ready = sem("pt_ready")
        pv_done = sem("pv_done")
        tree_step = sem("tree_step")
        recip_done = sem("recip_done")
        guard_done = sem("guard_done")
        scale_ready = sem("scale_ready")
        scale_turned = sem("scale_turned")
        scale_t_ready = sem("scale_t_ready")
        att_ready = sem("att_ready")
        oproj_done = sem("oproj_done")
        xb_ready = sem("xb_ready")
        y_ready = sem("y_ready")
        stats_done = sem("stats_done")
        moments_done = sem("moments_done")
        eps_added = sem("eps_added")
        rstd_ready = sem("rstd_ready")
        out_ready = sem("out_ready")
        stored = [sem(f"stored{i}") for i in range(2)]

        TREE = 7

        def has(b):
            return not isinstance(b, int) or 0 <= b < NB

        def wait(eng, semaphore, value):
            if not isinstance(value, int) or value > 0:
                eng.wait_ge(semaphore, value)

        def settle(eng):
            eng.nop(nofuse=True)

        def in_steps(eng, slot):
            for s in range(BODY):
                slot(0, s)
            with eng.Fori(1, STEPS - 1) as i:
                for s in range(BODY):
                    slot(i, s)
            for s in range(BODY):
                slot(STEPS - 1, s)
            slot(STEPS, 0)
            slot(STEPS, 1)

        def loaded(s):
            return (s // GRP) % 2

        block = ctx.enter_context(nc.Block())

        @block.sync
        def _(sp):
            sp.dma_start(x_t[:, 0], xt[0]).then_inc(xt_in[0], DMA)
            sp.dma_start(w_k[:], wk).then_inc(w_in["k"], DMA)
            sp.dma_start(w_q[:], wq).then_inc(w_in["q"], DMA)
            sp.dma_start(w_v[:], wv).then_inc(w_in["v"], DMA)
            sp.dma_start(bv_rows[:], bv.to_broadcast([P, HID])).then_inc(w_in["b"], DMA)
            sp.dma_start(adj_n[:, 0], adj[0]).then_inc(adj_in[0], DMA)
            sp.dma_start(x_t[:, 1], xt[1]).then_inc(xt_in[1], DMA)
            sp.dma_start(bo_rows[:], bo.to_broadcast([P, HID])).then_inc(w_in["b"], DMA)
            sp.dma_start(x_n[:, 0], xn[0]).then_inc(xn_in[0], DMA)
            sp.dma_start(w_o[:], wo).then_inc(w_in["o"], DMA)
            sp.dma_start(adj_n[:, 1], adj[1]).then_inc(adj_in[1], DMA)
            sp.dma_start(x_n[:, 1], xn[1]).then_inc(xn_in[1], DMA)

            def refill(i, half):
                g = i * 2 + half
                sp.wait_ge(vproj_done, (g - 1) * GRP)
                sp.dma_start(x_t[:, half], xt[g]).then_inc(xt_in[half], DMA)
                sp.wait_ge(biased, (g - 1) * GRP * KT)
                sp.dma_start(adj_n[:, half], adj[g]).then_inc(adj_in[half], DMA)
                sp.wait_ge(y_ready, (g - 1) * GRP)
                sp.dma_start(x_n[:, half], xn[g]).then_inc(xn_in[half], DMA)

            def store(i, half):
                g = i * 2 + half
                sp.wait_ge(out_ready, (g + 1) * GRP)
                sp.dma_start(out[g], out_n[:, half]).then_inc(stored[half], DMA)

            with sp.Fori(1, STEPS) as i:
                for half in range(2):
                    refill(i, half)
                    store(i - 1, half)
            for half in range(2):
                store(STEPS - 1, half)
            for half in range(2):
                sp.wait_ge(stored[half], DMA * STEPS)

        @block.gpsimd
        def _(pool):
            nc.gpsimd.memset(minus_half[:], -0.5)
            nc.gpsimd.memset(ident[:], 0.0).then_inc(ident_step, 1)
            pool.wait_ge(ident_step, 1)
            nc.gpsimd.affine_select(out=ident[:], in_=ident[:], compare_op=ALU.not_equal, fill=1.0, base=0,
                                    pattern=[[-1, P]], channel_multiplier=1).then_inc(ident_step, 1)
            nc.gpsimd.memset(k_diag[:, 1], 0.0).then_inc(diag_zeroed[1], 1)
            pool.wait_ge(w_in["b"], 2 * DMA)

            def sum_scores(b, par):
                wait(pool, biased, KT * b + KT)
                wait(pool, guard_done, b)
                width, src = P // 2, nscores[:, par]
                for n in range(TREE):
                    if n:
                        pool.wait_ge(tree_step, b * TREE + n)
                    at = P - 2 * width
                    nc.gpsimd.tensor_tensor(tree[:, :, at:at + width], src[:, :, 0:width],
                                            src[:, :, width:2 * width], ALU.add).then_inc(tree_step, 1)
                    src = tree[:, :, at:at + width]
                    width //= 2

            def slot(i, s):
                b = i * BODY + s
                half, t = loaded(s), s % GRP
                if has(b):
                    if t == 0:
                        pool.wait_ge(xn_in[half], (i + 1) * DMA)
                    nc.gpsimd.tensor_tensor(x_n[:, half, t], x_n[:, half, t], bo_rows[:],
                                            ALU.add).then_inc(xb_ready, 1)
                if has(b + 1):
                    sum_scores(b + 1, (s + 1) % 2)
                if has(b - 1):
                    par = (s - 1) % 2
                    pool.wait_ge(moments_done, b)
                    wait(pool, out_ready, b - 2)
                    settle(pool)
                    nc.gpsimd.tensor_scalar(var_eps[:], mean_var[:, par, 1:2], EPS, 1.0, ALU.add,
                                            ALU.mult).then_inc(eps_added, 1)
                    pool.wait_ge(eps_added, b)
                    nc.gpsimd.tensor_tensor(rstd[:, par:par + 1], var_eps[:], minus_half[:],
                                            ALU.pow).then_inc(rstd_ready, 1)

            sum_scores(0, 0)
            in_steps(pool, slot)

        @block.tensor
        def _(pe):
            def project(half, m, w, bank):
                for k in range(KT):
                    last = nc.tensor.matmul(mm_ps[bank][:, :], w[:, k, m * P:(m + 1) * P], x_t[:, half, k],
                                            start=(k == 0), stop=(k == KT - 1))
                last.then_inc(proj_done, 1)

            def score(half, t, m):
                nc.tensor.matmul(scores_ps[m][:], q_t[:, half, m, t * P:(t + 1) * P],
                                 k_diag[:, half, t, m], start=True, stop=True).then_inc(scores_done, 1)

            def values(half, t, bank):
                for k in range(KT):
                    last = nc.tensor.matmul(mm_ps[bank][:, 0:HID], x_t[:, half, k, t * P:(t + 1) * P],
                                            w_v[:, k], start=(k == 0), stop=(k == KT - 1))
                last.then_inc(vproj_done, 1)

            def turn(b, par, m):
                pe.wait_ge(probs_ready, KT * b + m + 1)
                wait(pe, pt_ready, KT * b + m - 1)
                bank = pt_ps[(KT * par + m) % 2]
                for j in range(HPT):
                    last = nc.tensor.transpose(bank[:, j], probs[:, par, m * HPT + j], ident[:])
                last.then_inc(turned, 1)

            def attend(b, par, m):
                if m == 0:
                    pe.wait_ge(v_ready, b + 1)
                    wait(pe, att_ready, b)
                pe.wait_ge(pt_ready, KT * b + m + 1)
                for j in range(HPT):
                    h = m * HPT + j
                    last = nc.tensor.matmul(att_ps[j * D:(j + 1) * D, m * P:(m + 1) * P],
                                            v_n[:, par, h * D:(h + 1) * D], probs_t[:, par, h],
                                            start=True, stop=True)
                last.then_inc(pv_done, 1)

            def turn_scale(b, par, bank):
                pe.wait_ge(scale_ready, b + 1)
                for m in range(KT):
                    tile = slice(m * P, (m + 1) * P)
                    last = nc.tensor.transpose(mm_ps[bank][:, tile], scale_n[:, par, tile], ident[:])
                last.then_inc(scale_turned, 1)

            def project_out(b, par, bank):
                pe.wait_ge(att_ready, b + 1)
                for k in range(KT):
                    last = nc.tensor.matmul(mm_ps[bank][:, 0:HID], att_t[:, par, k], w_o[:, k],
                                            start=(k == 0), stop=(k == KT - 1))
                last.then_inc(oproj_done, 1)

            def slot(i, s):
                b = i * BODY + s
                half, t, par = loaded(s), s % GRP, s % 2
                one, other = par, 1 - par
                gn = i * 2 + s // GRP + 1
                more = t < KT and has(b) and has(gn * GRP)
                if has(b + 1):
                    s1 = (s + 1) % BODY
                    half1, t1 = loaded(s1), s1 % GRP
                    if t1 == 0:
                        pe.wait_ge(q_ready, gn * KT)
                    for m in range(KT):
                        if t1 == 0:
                            pe.wait_ge(k_ready, gn * KT + m + 1)
                        pe.wait_ge(biased, KT * b + m + 1)
                        score(half1, t1, m)
                    wait(pe, scale_t_ready, b)
                    values(half1, t1, one)
                if has(b):
                    turn(b, par, 0)
                    turn(b, par, 1)
                    if more:
                        wait(pe, y_ready, b - 1)
                        if t == 0:
                            pe.wait_ge(xt_in[1 - half], (i + (s // GRP) + 1) * DMA)
                        project(1 - half, t, w_k, other)
                    attend(b, par, 0)
                    turn(b, par, 2)
                    if more:
                        pe.wait_ge(v_ready, b + 2)
                        project(1 - half, t, w_q, one)
                    attend(b, par, 1)
                    attend(b, par, 2)
                    if more:
                        pe.wait_ge(k_ready, gn * KT + t + 1)
                    else:
                        wait(pe, y_ready, b - 1)
                    turn_scale(b, par, other)
                if has(b - 1):
                    if more:
                        pe.wait_ge(q_ready, gn * KT + t + 1)
                    elif has(b + 1):
                        pe.wait_ge(v_ready, b + 2)
                    project_out(b - 1, 1 - par, one)

            pe.wait_ge(xt_in[0], DMA)
            pe.wait_ge(w_in["k"], DMA)
            for m in range(KT):
                if m:
                    pe.wait_ge(k_ready, m)
                project(0, m, w_k, 0)
                if m == 0:
                    pe.wait_ge(w_in["q"], DMA)
                else:
                    pe.wait_ge(q_ready, m)
                project(0, m, w_q, 1)
            for m in range(KT):
                pe.wait_ge(k_ready, m + 1)
                pe.wait_ge(q_ready, m + 1)
                score(0, 0, m)
            pe.wait_ge(w_in["v"], DMA)
            values(0, 0, 1)
            pe.wait_ge(v_ready, 1)
            pe.wait_ge(ident_step, 2)
            pe.wait_ge(w_in["o"], DMA)
            in_steps(pe, slot)

        @block.scalar
        def _(act):
            def softmax_top(b, par):
                for m in range(KT):
                    act.wait_ge(biased, KT * b + m + 1)
                    if m == 0:
                        wait(act, turned, KT * (b - 1))
                        wait(act, recip_done, b - 1)
                    for j in range(HPT):
                        h = m * HPT + j
                        last = nc.scalar.activation(probs[:, par, h], nscores[:, par, h], ACT.Exp,
                                                    bias=neg_max[:, par, h:h + 1], scale=-1.0,
                                                    accum_out=row_sum[:, par, h:h + 1])
                    last.then_inc(probs_ready, 1)

            def keep_k(g, half, m, bank):
                act.wait_ge(proj_done, g * 2 * KT + 2 * m + 1)
                if m == 0:
                    wait(act, scores_done, (g - 1) * GRP * KT)
                for j in range(HPT):
                    rows = slice(j * D, (j + 1) * D)
                    last = nc.scalar.activation(k_diag[rows, half, :, m, j],
                                                mm_ps[bank][rows, :].rearrange("p (g k) -> p g k", g=GRP),
                                                ACT.Copy)
                last.then_inc(k_ready, 1)

            def keep_q(g, half, m, bank):
                act.wait_ge(proj_done, g * 2 * KT + 2 * m + 2)
                nc.scalar.activation(q_t[:, half, m], mm_ps[bank][:], ACT.Copy,
                                     scale=0.5 * SCALE).then_inc(q_ready, 1)

            def slot(i, s):
                b = i * BODY + s
                t, par = s % GRP, s % 2
                gn = i * 2 + s // GRP + 1
                if has(b + 1):
                    softmax_top(b + 1, (s + 1) % 2)
                more = t < KT and has(b) and has(gn * GRP)
                if more:
                    keep_k(gn, 1 - loaded(s), t, 1 - par)
                    keep_q(gn, 1 - loaded(s), t, par)
                if has(b):
                    act.wait_ge(scale_turned, b + 1)
                    wait(act, att_ready, b - 1)
                    nc.scalar.activation(scale_t[:, par], mm_ps[1 - par][:, 0:HID],
                                         ACT.Copy).then_inc(scale_t_ready, 1)

            act.wait_ge(diag_zeroed[0], 1)
            act.wait_ge(diag_zeroed[1], 1)
            for m in range(KT):
                keep_k(0, 0, m, 0)
                keep_q(0, 0, m, 1)
            softmax_top(0, 0)
            in_steps(act, slot)

        @block.vector
        def _(dve):
            def bias_and_max(b, i, s, half, t, par):
                if t == 0:
                    dve.wait_ge(adj_in[half], (i + 1) * DMA)
                for m in range(KT):
                    dve.wait_ge(scores_done, KT * b + m + 1)
                    if m == 0:
                        wait(dve, probs_ready, KT * (b - 1))
                        wait(dve, tree_step, TREE * (b - 1))
                        wait(dve, guard_done, b - 1)
                    settle(dve)
                    for j in range(HPT):
                        h = m * HPT + j
                        last = nc.vector.tensor_tensor_reduce(
                            out=nscores[:, par, h], in0=scores_ps[m][:, j], in1=adj_n[:, half, t],
                            scale=-2.0, scalar=3.0e38, op0=ALU.add, op1=ALU.min,
                            accum_out=neg_max[:, par, h:h + 1])
                    last.then_inc(biased, 1)

            def keep_v(b, par, bank):
                dve.wait_ge(vproj_done, b + 1)
                wait(dve, pv_done, KT * (b - 1))
                nc.vector.tensor_tensor(v_n[:, par], mm_ps[bank][:, 0:HID], bv_rows[:],
                                        ALU.add).then_inc(v_ready, 1)

            def slot(i, s):
                b = i * BODY + s
                half, t, par = loaded(s), s % GRP, s % 2
                if has(b + 1):
                    s1 = (s + 1) % BODY
                    bias_and_max(b + 1, i + (s + 1) // BODY, s1, loaded(s1), s1 % GRP, s1 % 2)
                    keep_v(b + 1, s1 % 2, par)
                if has(b - 2):
                    p2, h2, t2 = (s - 2) % 2, loaded((s - 2) % BODY), (s - 2) % GRP
                    i2 = i + (s - 2) // BODY
                    dve.wait_ge(rstd_ready, b - 1)
                    if t2 == 0:
                        wait(dve, stored[h2], i2 * DMA)
                    nc.vector.tensor_scalar(out_n[:, h2, t2], y[:, p2], mean_var[:, p2, 0:1],
                                            rstd[:, p2:p2 + 1], ALU.subtract, ALU.mult).then_inc(out_ready, 1)
                if has(b):
                    for m in range(KT):
                        dve.wait_ge(turned, KT * b + m + 1)
                        if m == 0:
                            wait(dve, pv_done, KT * (b - 1))
                        nc.vector.tensor_copy(probs_t[:, par, m * HPT:(m + 1) * HPT],
                                              pt_ps[(KT * par + m) % 2][:]).then_inc(pt_ready, 1)
                    wait(dve, scale_ready, b)
                    nc.vector.reciprocal(recip[:], row_sum[:, par]).then_inc(recip_done, 1)
                    dve.wait_ge(tree_step, TREE * (b + 1))
                    nc.vector.scalar_tensor_tensor(
                        out=guard[:], in0=tree[:, :, P - 2], scalar=0.0, in1=neg_max[:, par],
                        op0=ALU.not_equal, op1=ALU.logical_or).then_inc(guard_done, 1)
                    dve.wait_ge(recip_done, b + 1)
                    dve.wait_ge(guard_done, b + 1)
                    wait(dve, scale_turned, b - 1)
                    nc.vector.tensor_tensor(scale_n[:, par].rearrange("p (h d) -> p h d", h=HEADS),
                                            recip[:].unsqueeze(2).to_broadcast([P, HEADS, D]),
                                            guard[:].unsqueeze(2).to_broadcast([P, HEADS, D]),
                                            ALU.mult).then_inc(scale_ready, 1)
                    dve.wait_ge(pv_done, KT * (b + 1))
                    dve.wait_ge(scale_t_ready, b + 1)
                    wait(dve, oproj_done, b - 1)
                    nc.vector.tensor_tensor(att_t[:, par], att_ps[:, 0:HID].rearrange("p (m q) -> p m q", m=KT),
                                            scale_t[:, par].rearrange("p (m q) -> p m q", m=KT),
                                            ALU.mult).then_inc(att_ready, 1)
                if has(b - 1):
                    p1, h1, t1 = (s - 1) % 2, loaded((s - 1) % BODY), (s - 1) % GRP
                    dve.wait_ge(oproj_done, b)
                    dve.wait_ge(xb_ready, b)
                    wait(dve, out_ready, b - 2)
                    nc.vector.tensor_tensor(y[:, p1], mm_ps[par][:, 0:HID], x_n[:, h1, t1],
                                            ALU.add).then_inc(y_ready, 1)
                    dve.wait_ge(y_ready, b)
                    nc.vector.bn_stats(stats[:, p1], y[:, p1]).then_inc(stats_done, 1)
                    dve.wait_ge(stats_done, b)
                    settle(dve)
                    nc.vector.bn_aggr(mean_var[:, p1], stats[:, p1]).then_inc(moments_done, 1)

            nc.vector.memset(k_diag[:, 0], 0.0).then_inc(diag_zeroed[0], 1)
            dve.wait_ge(w_in["b"], 2 * DMA)
            bias_and_max(0, 0, 0, 0, 0, 0)
            keep_v(0, 0, 1)
            in_steps(dve, slot)


def kernel(x, adj, L0_gnn_Wq, L0_gnn_Wk, L0_gnn_Wv, L0_gnn_bv, L0_gnn_Wo, L0_gnn_bo):
    import numpy as np
    import concourse.bacc as bacc
    from concourse.bass_utils import run_bass_kernel_spmd

    def tokens_first(a):
        return np.ascontiguousarray(a.reshape(NG, GRP, P, -1).transpose(0, 2, 1, 3))

    def channels_first(w):
        return np.ascontiguousarray(w.T.reshape(KT, P, -1).transpose(1, 0, 2))

    x, adj = np.asarray(x), np.asarray(adj)
    arrays = {
        "xt": np.ascontiguousarray(x.reshape(NG, GRP * P, KT, P).transpose(0, 3, 2, 1)),
        "xn": tokens_first(x),
        "adj": tokens_first(adj),
        "wq": channels_first(np.asarray(L0_gnn_Wq)),
        "wk": channels_first(np.asarray(L0_gnn_Wk)),
        "wv": channels_first(np.asarray(L0_gnn_Wv)),
        "wo": channels_first(np.asarray(L0_gnn_Wo)),
        "bv": np.asarray(L0_gnn_bv).reshape(1, HID),
        "bo": np.asarray(L0_gnn_bo).reshape(1, HID),
    }
    nc = bacc.Bacc("TRN2", target_bir_lowering=False, num_devices=1)
    aps = {n: nc.dram_tensor(n, a.shape, mybir.dt.from_np(a.dtype), kind="ExternalInput").ap()
           for n, a in arrays.items()}
    aps["out"] = nc.dram_tensor("out", (NG, P, GRP, HID), F32, kind="ExternalOutput").ap()
    build(nc, **aps)
    got = run_bass_kernel_spmd(nc, [arrays], core_ids=[0]).results[0]["out"]
    return np.ascontiguousarray(np.asarray(got).transpose(0, 2, 1, 3)).reshape(NB, P, HID)
```

```python
from contextlib import ExitStack

import concourse.bass as bass
from concourse import mybir
from concourse.alu_op_type import AluOpType as ALU

ACT = mybir.ActivationFunctionType
F32 = mybir.dt.float32
F32R = mybir.dt.float32r

P = 128
NB = 64
HID = 384
HEADS = 12
D = HID // HEADS
KT = HID // P
HPT = P // D
GRP = 4
NG = NB // GRP
BODY = 2 * GRP
STEPS = NB // BODY
TILES = 2 * KT
EPS = 1e-5
SCALE = float(HID) ** -0.5
DMA = 16
HI, LO = 0, 1
TERMS = ((HI, HI), (HI, LO), (LO, HI))
TREE = 3
REST = P >> TREE


def build(nc, xt, xn, adj, wq, wk, wv, wo, bv, bo, out):
    with ExitStack() as ctx:
        def sb(name, shape, dt=F32):
            return ctx.enter_context(nc.sbuf_tensor(name, shape, dt))

        def ps(name, shape):
            return ctx.enter_context(nc.psum_tensor(name, shape, F32))

        def sem(name):
            return ctx.enter_context(nc.semaphore(name))

        w_k = sb("w_k", [P, 2, KT, HID], F32R)
        w_q = sb("w_q", [P, 2, KT, HID], F32R)
        w_v = sb("w_v", [P, 2, KT, HID], F32R)
        w_o = sb("w_o", [P, 2, KT, HID], F32R)
        bv_rows = sb("bv_rows", [P, HID])
        bo_rows = sb("bo_rows", [P, HID])
        ident = sb("ident", [P, P])
        minus_half = sb("minus_half", [P, 1])
        x_raw = sb("x_raw", [P, KT, GRP * P])
        x_t = sb("x_t", [P, 2, 2, KT, GRP * P], F32R)
        q_t = sb("q_t", [P, 2, 2, KT, GRP * P], F32R)
        k_t = sb("k_t", [P, 2, 2, KT, GRP * P], F32R)
        k_diag = sb("k_diag", [P, 2, 2, KT, HPT, P], F32R)
        x_n = sb("x_n", [P, 2, 2, HID])
        adj_n = sb("adj_n", [P, 2, 2, P])
        v_n = sb("v_n", [P, 2, HID])
        nscores = sb("nscores", [P, 2, HEADS, P])
        probs = sb("probs", [P, 2, HEADS, P])
        probs_t = sb("probs_t", [P, HEADS, P])
        neg_max = sb("neg_max", [P, 2, HEADS])
        row_sum = sb("row_sum", [P, 2, HEADS])
        tree = sb("tree", [P, HEADS, P // 2])
        total = sb("total", [P, HEADS])
        recip = sb("recip", [P, HEADS])
        guard = sb("guard", [P, HEADS])
        scale_n = sb("scale_n", [P, HID])
        scale_t = sb("scale_t", [P, HID])
        att = sb("att", [P, HID])
        att_t = sb("att_t", [P, 2, KT, P], F32R)
        y = sb("y", [P, 2, HID])
        stats = sb("stats", [P, 6])
        mean_var = sb("mean_var", [P, 2, 2])
        var_eps = sb("var_eps", [P, 1])
        rstd = sb("rstd", [P, 2])
        out_n = sb("out_n", [P, 2, 2, HID])

        def as_weight(buf):
            return buf.rearrange("p h q -> p (h q)")[:, 0:KT * HID].rearrange("p (k n) -> p k n", k=KT)
        raw = [as_weight(buf[:, half]) for buf in (nscores, probs) for half in range(2)]

        scores_ps = [ps(f"scores_ps{m}", [P, HPT, P]) for m in range(KT)]
        pt_ps = [ps(f"pt_ps{i}", [P, HPT, P]) for i in range(2)]
        att_ps = ps("att_ps", [P, 512])
        mm_ps = [ps(f"mm_ps{i}", [P, 512]) for i in range(2)]

        wk_in, wq_in, wv_in, wo_in, bias_in = (sem(n) for n in ("wk_in", "wq_in", "wv_in", "wo_in", "bias_in"))
        xt_in = sem("xt_in")
        xn_in = [sem(f"xn_in{i}") for i in range(2)]
        adj_in = [sem(f"adj_in{i}") for i in range(2)]
        diag_in = [sem(f"diag_in{i}") for i in range(2)]
        stored = [sem(f"stored{i}") for i in range(2)]
        ident_step = sem("ident_step")
        diag_zeroed = sem("diag_zeroed")
        w_high = sem("w_high")
        w_split = sem("w_split")
        x_high = sem("x_high")
        x_split = sem("x_split")
        x_split_on = sem("x_split_on")
        proj_done = sem("proj_done")
        kept_high = sem("kept_high")
        kept = sem("kept")
        scores_done = sem("scores_done")
        biased = sem("biased")
        vproj_done = sem("vproj_done")
        v_ready = sem("v_ready")
        probs_ready = sem("probs_ready")
        turned = sem("turned")
        pt_ready = sem("pt_ready")
        pt_last = sem("pt_last")
        pv_done = sem("pv_done")
        tree_step = sem("tree_step")
        total_done = sem("total_done")
        recip_done = sem("recip_done")
        guard_done = sem("guard_done")
        scale_ready = sem("scale_ready")
        scale_turned = sem("scale_turned")
        scale_t_ready = sem("scale_t_ready")
        att_done = sem("att_done")
        att_high = sem("att_high")
        att_split = sem("att_split")
        oproj_done = sem("oproj_done")
        xb_ready = sem("xb_ready")
        y_ready = sem("y_ready")
        stats_done = sem("stats_done")
        moments_done = sem("moments_done")
        eps_added = sem("eps_added")
        rstd_ready = sem("rstd_ready")
        out_ready = sem("out_ready")

        def has(b):
            return not isinstance(b, int) or 0 <= b < NB

        def wait(eng, semaphore, value):
            if not isinstance(value, int) or value > 0:
                eng.wait_ge(semaphore, value)

        def settle(eng):
            eng.nop(nofuse=True)

        def in_steps(eng, slot):
            for s in range(BODY):
                slot(0, s)
            with eng.Fori(1, STEPS - 1) as i:
                for s in range(BODY):
                    slot(i, s)
            for s in range(BODY):
                slot(STEPS - 1, s)
            slot(STEPS, 0)
            slot(STEPS, 1)

        def graph_half(s):
            return s % 2

        def pair_half(s):
            return (s // 2) % 2

        def group_half(s):
            return (s // GRP) % 2

        def projects(i, s):
            return s % GRP < KT and has(i * BODY + s) and has((i * 2 + s // GRP + 1) * GRP)

        block = ctx.enter_context(nc.Block())

        @block.sync
        def _(sp):
            def place(b, group, s):
                half, t = graph_half(s), s % GRP
                sp.wait_ge(kept, group * TILES + KT)
                wait(sp, scores_done, KT * (b - 1))
                for j in range(HPT):
                    rows = slice(j * D, (j + 1) * D)
                    sp.dma_start(k_diag[rows, half, :, :, j].bitcast(F32),
                                 k_t[rows, group_half(s), :, :, t * P:(t + 1) * P].bitcast(F32)
                                 ).then_inc(diag_in[half], DMA)

            sp.dma_start(x_raw[:], xt[0]).then_inc(xt_in, DMA)
            sp.dma_start(raw[0], wk).then_inc(wk_in, DMA)
            sp.dma_start(raw[1], wq).then_inc(wq_in, DMA)
            sp.dma_start(raw[2], wv).then_inc(wv_in, DMA)
            sp.dma_start(adj_n[:, 0], adj[0]).then_inc(adj_in[0], DMA)
            sp.dma_start(bv_rows[:], bv.to_broadcast([P, HID])).then_inc(bias_in, DMA)
            sp.dma_start(bo_rows[:], bo.to_broadcast([P, HID])).then_inc(bias_in, DMA)
            sp.wait_ge(x_split, 1)
            sp.dma_start(x_raw[:], xt[1]).then_inc(xt_in, DMA)
            sp.dma_start(raw[3], wo).then_inc(wo_in, DMA)
            sp.wait_ge(diag_zeroed, 2)
            place(0, 0, 0)
            place(1, 0, 1)
            sp.dma_start(x_n[:, 0], xn[0]).then_inc(xn_in[0], DMA)
            sp.dma_start(adj_n[:, 1], adj[1]).then_inc(adj_in[1], DMA)
            sp.dma_start(x_n[:, 1], xn[1]).then_inc(xn_in[1], DMA)

            def slot(i, s):
                b = i * BODY + s
                if has(b + 2):
                    place(b + 2, i * 2 + (s + 2) // GRP, (s + 2) % BODY)
                if s % GRP == 0 and has((i * 2 + s // GRP + 2) * GRP):
                    g = i * 2 + s // GRP + 2
                    sp.wait_ge(x_split_on, g - 1)
                    sp.dma_start(x_raw[:], xt[g]).then_inc(xt_in, DMA)
                if s % 2:
                    pair = i * (BODY // 2) + s // 2
                    if has((pair + 2) * 2):
                        sp.wait_ge(biased, KT * (b + 1))
                        sp.dma_start(adj_n[:, pair_half(s)], adj[pair + 2]).then_inc(adj_in[pair_half(s)], DMA)
                    if has((pair + 1) * 2) and has(b - 2):
                        sp.wait_ge(y_ready, b - 1)
                        sp.dma_start(x_n[:, pair_half(s + 2)], xn[pair + 1]).then_inc(xn_in[pair_half(s + 2)], DMA)
                elif has(b - 4):
                    pair = i * (BODY // 2) + (s - 4) // 2
                    sp.wait_ge(out_ready, b - 2)
                    sp.dma_start(out[pair], out_n[:, pair_half(s - 4)]).then_inc(stored[pair_half(s - 4)], DMA)

            in_steps(sp, slot)
            last = NB // 2 - 1
            sp.wait_ge(out_ready, NB)
            sp.dma_start(out[last], out_n[:, last % 2]).then_inc(stored[last % 2], DMA)
            for half in range(2):
                sp.wait_ge(stored[half], DMA * (NB // 4))

        @block.gpsimd
        def _(pool):
            for half in range(2):
                nc.gpsimd.memset(k_diag[:, half].bitcast(F32), 0.0).then_inc(diag_zeroed, 1)
            nc.gpsimd.memset(minus_half[:], -0.5)
            nc.gpsimd.memset(ident[:], 0.0).then_inc(ident_step, 1)
            pool.wait_ge(ident_step, 1)
            nc.gpsimd.affine_select(out=ident[:], in_=ident[:], compare_op=ALU.not_equal, fill=1.0, base=0,
                                    pattern=[[-1, P]], channel_multiplier=1).then_inc(ident_step, 1)
            pool.wait_ge(bias_in, 2 * DMA)

            def sum_scores(b, half):
                wait(pool, biased, KT * b + KT)
                wait(pool, total_done, b)
                src = nscores[:, half]
                for n in range(TREE):
                    width = P >> (n + 1)
                    if n:
                        pool.wait_ge(tree_step, b * TREE + n)
                    nc.gpsimd.tensor_tensor(tree[:, :, 0:width], src[:, :, 0:width],
                                            src[:, :, width:2 * width], ALU.add).then_inc(tree_step, 1)
                    src = tree

            def split_x_low(g, half):
                pool.wait_ge(x_high, g + 1)
                nc.gpsimd.tensor_tensor(x_t[:, half, LO], x_raw[:], x_t[:, half, HI].bitcast(F32),
                                        ALU.subtract).then_inc(x_split_on, 1)

            def spread_scale(b):
                pool.wait_ge(recip_done, b + 1)
                pool.wait_ge(guard_done, b + 1)
                wait(pool, scale_turned, b)
                nc.gpsimd.tensor_tensor(scale_n[:].rearrange("p (h d) -> p h d", h=HEADS),
                                        recip[:].unsqueeze(2).to_broadcast([P, HEADS, D]),
                                        guard[:].unsqueeze(2).to_broadcast([P, HEADS, D]),
                                        ALU.mult).then_inc(scale_ready, 1)

            def slot(i, s):
                b = i * BODY + s
                if has(b):
                    row = x_n[:, pair_half(s), s % 2]
                    if s % 2 == 0:
                        pool.wait_ge(xn_in[pair_half(s)], (i * 2 + s // 4 + 1) * DMA)
                    nc.gpsimd.tensor_tensor(row, row, bo_rows[:], ALU.add).then_inc(xb_ready, 1)
                if has(b + 1):
                    sum_scores(b + 1, graph_half(s + 1))
                    spread_scale(b + 1)
                if has(b - 1):
                    half = graph_half(s - 1)
                    pool.wait_ge(moments_done, b)
                    wait(pool, out_ready, b - 2)
                    settle(pool)
                    nc.gpsimd.tensor_scalar(var_eps[:], mean_var[:, half, 1:2], EPS, 1.0, ALU.add,
                                            ALU.mult).then_inc(eps_added, 1)
                    pool.wait_ge(eps_added, b)
                    nc.gpsimd.tensor_tensor(rstd[:, half:half + 1], var_eps[:], minus_half[:],
                                            ALU.pow).then_inc(rstd_ready, 1)
                gn = i * 2 + s // GRP + 1
                if s % GRP == KT - 1 and has((gn + 1) * GRP):
                    split_x_low(gn + 1, group_half(s))

            split_x_low(1, 1)
            sum_scores(0, 0)
            spread_scale(0)
            in_steps(pool, slot)

        @block.tensor
        def _(pe):
            def project(half, tile, bank):
                w = (w_k, w_q)[tile // KT]
                cols = slice(tile % KT * P, (tile % KT + 1) * P)
                for k in range(KT):
                    for n, (a, c) in enumerate(TERMS):
                        last = nc.tensor.matmul(mm_ps[bank][:, :], w[:, a, k, cols], x_t[:, half, c, k],
                                                start=(k == 0 and n == 0),
                                                stop=(k == KT - 1 and n == len(TERMS) - 1))
                last.then_inc(proj_done, 1)

            def score(s, m):
                cols = slice(s % GRP * P, (s % GRP + 1) * P)
                for n, (a, c) in enumerate(TERMS):
                    last = nc.tensor.matmul(scores_ps[m][:], q_t[:, group_half(s), a, m, cols],
                                            k_diag[:, graph_half(s), c, m],
                                            start=(n == 0), stop=(n == len(TERMS) - 1))
                last.then_inc(scores_done, 1)

            def values(s, bank):
                cols = slice(s % GRP * P, (s % GRP + 1) * P)
                for k in range(KT):
                    for n, (a, c) in enumerate(TERMS):
                        last = nc.tensor.matmul(mm_ps[bank][:, 0:HID], x_t[:, group_half(s), a, k, cols],
                                                w_v[:, c, k], start=(k == 0 and n == 0),
                                                stop=(k == KT - 1 and n == len(TERMS) - 1))
                last.then_inc(vproj_done, 1)

            def turn(b, half, m):
                pe.wait_ge(probs_ready, KT * b + m + 1)
                if m == 2:
                    pe.wait_ge(pt_ready, 2 * b + 1)
                elif m == 1:
                    wait(pe, pt_last, b)
                else:
                    wait(pe, pt_ready, 2 * b)
                bank = pt_ps[(KT * half + m) % 2]
                for j in range(HPT):
                    last = nc.tensor.transpose(bank[:, j], probs[:, half, m * HPT + j], ident[:])
                last.then_inc(turned, 1)

            def attend(b, half, m):
                if m == 0:
                    pe.wait_ge(v_ready, b + 1)
                    wait(pe, att_done, b)
                if m < 2:
                    pe.wait_ge(pt_ready, 2 * b + m + 1)
                else:
                    pe.wait_ge(pt_last, b + 1)
                for j in range(HPT):
                    h = m * HPT + j
                    last = nc.tensor.matmul(att_ps[j * D:(j + 1) * D, m * P:(m + 1) * P],
                                            v_n[:, half, h * D:(h + 1) * D], probs_t[:, h],
                                            start=True, stop=True)
                last.then_inc(pv_done, 1)

            def turn_scale(b, bank):
                pe.wait_ge(scale_ready, b + 1)
                for m in range(KT):
                    tile = slice(m * P, (m + 1) * P)
                    last = nc.tensor.transpose(mm_ps[bank][:, tile], scale_n[:, tile], ident[:])
                last.then_inc(scale_turned, 1)

            def project_out(b, bank):
                pe.wait_ge(att_split, b + 1)
                for k in range(KT):
                    for n, (a, c) in enumerate(TERMS):
                        last = nc.tensor.matmul(mm_ps[bank][:, 0:HID], att_t[:, a, k], w_o[:, c, k],
                                                start=(k == 0 and n == 0),
                                                stop=(k == KT - 1 and n == len(TERMS) - 1))
                last.then_inc(oproj_done, 1)

            def slot(i, s):
                b = i * BODY + s
                t, half = s % GRP, graph_half(s)
                one, other = half, 1 - half
                gn = i * 2 + s // GRP + 1
                more = projects(i, s)
                s1 = (s + 1) % BODY
                if has(b):
                    turn(b, half, 0)
                    turn(b, half, 1)
                if has(b + 1):
                    if has(b - 1) and projects(i, s - 1):
                        pe.wait_ge(kept, gn * TILES + 2 * t)
                    else:
                        wait(pe, scale_t_ready, b)
                    values(s1, one)
                if has(b + 1):
                    if s1 % GRP == 0:
                        pe.wait_ge(kept, gn * TILES + TILES)
                    pe.wait_ge(diag_in[1 - half], (i * (BODY // 2) + (s + 1) // 2 + 1) * HPT * DMA)
                    for m in range(KT):
                        pe.wait_ge(biased, KT * b + m + 1)
                        score(s1, m)
                if has(b):
                    wait(pe, y_ready, b - 1)
                    turn_scale(b, other)
                if more:
                    pe.wait_ge(v_ready, b + 2)
                    if t == 0:
                        pe.wait_ge(x_split_on, gn)
                    project(1 - group_half(s), 2 * t, one)
                    attend(b, half, 0)
                    turn(b, half, 2)
                    pe.wait_ge(scale_t_ready, b + 1)
                    project(1 - group_half(s), 2 * t + 1, other)
                    attend(b, half, 1)
                    attend(b, half, 2)
                    if has(b - 1):
                        pe.wait_ge(kept, gn * TILES + 2 * t + 1)
                        project_out(b - 1, one)
                else:
                    if has(b - 1):
                        if has(b + 1):
                            pe.wait_ge(v_ready, b + 2)
                        else:
                            wait(pe, scale_t_ready, min(b, NB))
                        project_out(b - 1, one)
                    if has(b):
                        attend(b, half, 0)
                        turn(b, half, 2)
                        attend(b, half, 1)
                        attend(b, half, 2)

            pe.wait_ge(x_split, 1)
            for tile in range(TILES):
                if tile % KT == 0:
                    pe.wait_ge(w_split, tile // KT + 1)
                wait(pe, kept, tile - 1)
                project(0, tile, tile % 2)
            pe.wait_ge(kept, TILES)
            pe.wait_ge(w_split, 3)
            values(0, 1)
            pe.wait_ge(diag_in[0], HPT * DMA)
            for m in range(KT):
                score(0, m)
            pe.wait_ge(v_ready, 1)
            pe.wait_ge(ident_step, 2)
            pe.wait_ge(w_split, 4)
            in_steps(pe, slot)

        @block.scalar
        def _(act):
            def softmax_top(b, half, m):
                act.wait_ge(biased, KT * b + m + 1)
                if m == 0:
                    wait(act, turned, KT * (b - 1))
                    wait(act, recip_done, b - 1)
                for j in range(HPT):
                    h = m * HPT + j
                    last = nc.scalar.activation(probs[:, half, h], nscores[:, half, h], ACT.Exp,
                                                bias=neg_max[:, half, h:h + 1], scale=-1.0,
                                                accum_out=row_sum[:, half, h:h + 1])
                last.then_inc(probs_ready, 1)

            def keep_high(g, half, tile, bank):
                act.wait_ge(proj_done, g * TILES + tile + 1)
                if tile == 0:
                    wait(act, scores_done, (g - 1) * GRP * KT)
                dst, scale = ((k_t, 1.0), (q_t, 0.5 * SCALE))[tile // KT]
                nc.scalar.activation(dst[:, half, HI, tile % KT], mm_ps[bank][:], ACT.Copy,
                                     scale=scale).then_inc(kept_high, 1)

            def split_x_high(g, half):
                act.wait_ge(xt_in, (g + 1) * DMA)
                wait(act, vproj_done, (g - 1) * GRP)
                nc.scalar.activation(x_t[:, half, HI], x_raw[:], ACT.Copy).then_inc(x_high, 1)

            def slot(i, s):
                b = i * BODY + s
                t, half = s % GRP, graph_half(s)
                one, other = half, 1 - half
                gn = i * 2 + s // GRP + 1
                if has(b - 1):
                    act.wait_ge(att_done, b)
                    wait(act, oproj_done, b - 1)
                    nc.scalar.activation(att_t[:, HI].rearrange("p m q -> p (m q)"), att[:],
                                         ACT.Copy).then_inc(att_high, 1)
                if has(b + 1):
                    softmax_top(b + 1, 1 - half, 0)
                if has(b):
                    act.wait_ge(scale_turned, b + 1)
                    wait(act, att_done, b)
                    nc.scalar.activation(scale_t[:], mm_ps[other][:, 0:HID], ACT.Copy).then_inc(scale_t_ready, 1)
                if has(b + 1):
                    softmax_top(b + 1, 1 - half, 1)
                if projects(i, s):
                    keep_high(gn, 1 - group_half(s), 2 * t, one)
                if has(b):
                    act.wait_ge(turned, KT * b + KT)
                    wait(act, pv_done, KT * b)
                    nc.scalar.activation(probs_t[:, 2 * HPT:], pt_ps[(KT * half + 2) % 2][:],
                                         ACT.Copy).then_inc(pt_last, 1)
                if has(b + 1):
                    softmax_top(b + 1, 1 - half, 2)
                if projects(i, s):
                    keep_high(gn, 1 - group_half(s), 2 * t + 1, other)
                if t == KT - 1 and has((gn + 1) * GRP):
                    split_x_high(gn + 1, group_half(s))

            split_x_high(0, 0)
            for n, (w, loaded) in enumerate(((w_k, wk_in), (w_q, wq_in), (w_v, wv_in), (w_o, wo_in))):
                act.wait_ge(loaded, DMA)
                nc.scalar.activation(w[:, HI], raw[n], ACT.Copy).then_inc(w_high, 1)
            for tile in range(TILES):
                keep_high(0, 0, tile, tile % 2)
            split_x_high(1, 1)
            act.wait_ge(w_split, 4)
            for m in range(KT):
                softmax_top(0, 0, m)
            in_steps(act, slot)

        @block.vector
        def _(dve):
            def bias_and_max(b, i, s):
                half = graph_half(s)
                if s % 2 == 0:
                    dve.wait_ge(adj_in[pair_half(s)], (i * 2 + s // 4 + 1) * DMA)
                for m in range(KT):
                    dve.wait_ge(scores_done, KT * b + m + 1)
                    if m == 0:
                        wait(dve, probs_ready, KT * (b - 1))
                        wait(dve, tree_step, TREE * (b - 1))
                        wait(dve, guard_done, b - 1)
                    settle(dve)
                    for j in range(HPT):
                        h = m * HPT + j
                        last = nc.vector.tensor_tensor_reduce(
                            out=nscores[:, half, h], in0=scores_ps[m][:, j], in1=adj_n[:, pair_half(s), s % 2],
                            scale=-2.0, scalar=3.0e38, op0=ALU.add, op1=ALU.min,
                            accum_out=neg_max[:, half, h:h + 1])
                    last.then_inc(biased, 1)

            def keep_v(b, half, bank):
                dve.wait_ge(vproj_done, b + 1)
                wait(dve, pv_done, KT * (b - 1))
                nc.vector.tensor_tensor(v_n[:, half], mm_ps[bank][:, 0:HID], bv_rows[:],
                                        ALU.add).then_inc(v_ready, 1)

            def keep_low(g, half, tile, bank):
                dve.wait_ge(kept_high, g * TILES + tile + 1)
                dst, scale = ((k_t, 1.0), (q_t, 0.5 * SCALE))[tile // KT]
                nc.vector.scalar_tensor_tensor(
                    out=dst[:, half, LO, tile % KT], in0=mm_ps[bank][:], scalar=scale,
                    in1=dst[:, half, HI, tile % KT].bitcast(F32), op0=ALU.mult,
                    op1=ALU.subtract).then_inc(kept, 1)

            def find_scale(b, half):
                if has(b):
                    wait(dve, scale_ready, b)
                    dve.wait_ge(probs_ready, KT * (b + 1))
                    nc.vector.reciprocal(recip[:], row_sum[:, half]).then_inc(recip_done, 1)
                    dve.wait_ge(tree_step, TREE * (b + 1))
                    nc.vector.reduce_sum(total[:], tree[:, :, 0:REST], axis=mybir.AxisListType.X
                                         ).then_inc(total_done, 1)
                    dve.wait_ge(total_done, b + 1)
                    nc.vector.scalar_tensor_tensor(
                        out=guard[:], in0=total[:], scalar=0.0, in1=neg_max[:, half],
                        op0=ALU.not_equal, op1=ALU.logical_or).then_inc(guard_done, 1)

            def attention_low(b):
                if has(b):
                    dve.wait_ge(att_high, b + 1)
                    nc.vector.tensor_tensor(att_t[:, LO].rearrange("p m q -> p (m q)"), att[:],
                                            att_t[:, HI].rearrange("p m q -> p (m q)").bitcast(F32),
                                            ALU.subtract).then_inc(att_split, 1)

            def normalise(b):
                if has(b):
                    dve.wait_ge(pv_done, KT * (b + 1))
                    dve.wait_ge(scale_t_ready, b + 1)
                    wait(dve, att_split, b)
                    nc.vector.tensor_tensor(att[:], att_ps[:, 0:HID], scale_t[:],
                                            ALU.mult).then_inc(att_done, 1)

            def residual(b, s, bank):
                if has(b - 1):
                    half = graph_half(s - 1)
                    dve.wait_ge(oproj_done, b)
                    dve.wait_ge(xb_ready, b)
                    wait(dve, out_ready, b - 2)
                    nc.vector.tensor_tensor(y[:, half], mm_ps[bank][:, 0:HID],
                                            x_n[:, pair_half(s - 1), (s - 1) % 2], ALU.add).then_inc(y_ready, 1)
                    dve.wait_ge(y_ready, b)
                    nc.vector.bn_stats(stats[:], y[:, half]).then_inc(stats_done, 1)
                    dve.wait_ge(stats_done, b)
                    settle(dve)
                    nc.vector.bn_aggr(mean_var[:, half], stats[:]).then_inc(moments_done, 1)

            def slot(i, s):
                b = i * BODY + s
                t, half = s % GRP, graph_half(s)
                one, other = half, 1 - half
                gn = i * 2 + s // GRP + 1
                if not projects(i, s):
                    attention_low(b - 1)
                if has(b):
                    for m in range(2):
                        dve.wait_ge(turned, KT * b + m + 1)
                        if m == 0:
                            wait(dve, pv_done, KT * b)
                        nc.vector.tensor_copy(probs_t[:, m * HPT:(m + 1) * HPT],
                                              pt_ps[(KT * half + m) % 2][:]).then_inc(pt_ready, 1)
                if has(b + 1):
                    keep_v(b + 1, 1 - half, one)
                    bias_and_max(b + 1, i + (s + 1) // BODY, (s + 1) % BODY)
                if projects(i, s):
                    attention_low(b - 1)
                if has(b - 2):
                    pair, n = pair_half(s - 2), s % 2
                    dve.wait_ge(rstd_ready, b - 1)
                    if n == 0:
                        wait(dve, stored[pair], (i * 2 + (s - 2) // 4) * DMA)
                    nc.vector.tensor_scalar(out_n[:, pair, n], y[:, half], mean_var[:, half, 0:1],
                                            rstd[:, half:half + 1], ALU.subtract, ALU.mult).then_inc(out_ready, 1)
                if projects(i, s):
                    keep_low(gn, 1 - group_half(s), 2 * t, one)
                    keep_low(gn, 1 - group_half(s), 2 * t + 1, other)
                    find_scale(b + 1, 1 - half)
                    normalise(b)
                    residual(b, s, one)
                else:
                    residual(b, s, one)
                    normalise(b)
                    find_scale(b + 1, 1 - half)

            dve.wait_ge(x_high, 1)
            nc.vector.tensor_tensor(x_t[:, 0, LO], x_raw[:], x_t[:, 0, HI].bitcast(F32),
                                    ALU.subtract).then_inc(x_split, 1)
            for n, w in enumerate((w_k, w_q, w_v, w_o)):
                dve.wait_ge(w_high, n + 1)
                nc.vector.tensor_tensor(w[:, LO], raw[n], w[:, HI].bitcast(F32),
                                        ALU.subtract).then_inc(w_split, 1)
            for tile in range(TILES):
                keep_low(0, 0, tile, tile % 2)
            dve.wait_ge(bias_in, 2 * DMA)
            dve.wait_ge(w_split, 2)
            keep_v(0, 0, 1)
            bias_and_max(0, 0, 0)
            find_scale(0, 0)
            in_steps(dve, slot)


def kernel(x, adj, L0_gnn_Wq, L0_gnn_Wk, L0_gnn_Wv, L0_gnn_bv, L0_gnn_Wo, L0_gnn_bo):
    import numpy as np
    import concourse.bacc as bacc
    from concourse.bass_utils import run_bass_kernel_spmd

    def tokens_first(a):
        return np.ascontiguousarray(a.reshape(NB // 2, 2, P, -1).transpose(0, 2, 1, 3))

    def channels_first(w):
        return np.ascontiguousarray(w.T.reshape(KT, P, -1).transpose(1, 0, 2))

    x, adj = np.asarray(x), np.asarray(adj)
    arrays = {
        "xt": np.ascontiguousarray(x.reshape(NG, GRP * P, KT, P).transpose(0, 3, 2, 1)),
        "xn": tokens_first(x),
        "adj": tokens_first(adj),
        "wq": channels_first(np.asarray(L0_gnn_Wq)),
        "wk": channels_first(np.asarray(L0_gnn_Wk)),
        "wv": channels_first(np.asarray(L0_gnn_Wv)),
        "wo": channels_first(np.asarray(L0_gnn_Wo)),
        "bv": np.asarray(L0_gnn_bv).reshape(1, HID),
        "bo": np.asarray(L0_gnn_bo).reshape(1, HID),
    }
    nc = bacc.Bacc("TRN2", target_bir_lowering=False, num_devices=1)
    aps = {n: nc.dram_tensor(n, a.shape, mybir.dt.from_np(a.dtype), kind="ExternalInput").ap()
           for n, a in arrays.items()}
    aps["out"] = nc.dram_tensor("out", (NB // 2, P, 2, HID), F32, kind="ExternalOutput").ap()
    build(nc, **aps)
    got = run_bass_kernel_spmd(nc, [arrays], core_ids=[0]).results[0]["out"]
    return np.ascontiguousarray(np.asarray(got).transpose(0, 2, 1, 3)).reshape(NB, P, HID)
```
